# Optimizing a Trainium2 kernel written in Bass

```python
import numpy as np
import jax
import jax.numpy as jnp

def _softmax(x, axis=-1):
    return jax.nn.softmax(x, axis=axis)

def _gelu(x):
    return jax.nn.gelu(x, approximate=True)

def _silu(x):
    return jax.nn.silu(x)

def _sigmoid(x):
    return jax.nn.sigmoid(x)

def _layernorm(x, axis=-1, eps=1e-05):
    m = jnp.mean(x, axis=axis, keepdims=True)
    v = jnp.var(x, axis=axis, keepdims=True)
    return (x - m) / jnp.sqrt(v + eps)

def _scatter_add(tgt, idx, src, axis=0):
    return tgt.at[idx].add(src)

def _segment_sum(src, seg, n):
    return jax.ops.segment_sum(src, seg, n)
kernel_name = 'mk_dlrm_tower_d1_rec_r8_38ba11'

def setup_inputs(seed: int=0):
    np.random.seed(seed)
    _w = jnp.asarray

    def _rec_inputs():
        import jax
        import jax.numpy as jnp
        _tk = jax.random.key(seed)
        ids = jnp.stack([jax.random.randint(jax.random.fold_in(_tk, 200 + f), (2048,), 0, v, jnp.int32) for f, v in enumerate([1250, 125000, 12500, 12500, 1000, 12500, 1250, 1250, 1000, 1250, 1000, 12500, 1000, 1000, 1250, 12500, 1250, 12500, 1250, 1250, 12500, 1000, 12500, 1250, 1250, 1000])], axis=1)
        tbl_0 = 0.05 * jax.random.normal(jax.random.fold_in(_tk, 500 + 0), (1250, 128), jnp.float32)
        tbl_1 = 0.05 * jax.random.normal(jax.random.fold_in(_tk, 500 + 1), (125000, 128), jnp.float32)
        tbl_2 = 0.05 * jax.random.normal(jax.random.fold_in(_tk, 500 + 2), (12500, 128), jnp.float32)
        tbl_3 = 0.05 * jax.random.normal(jax.random.fold_in(_tk, 500 + 3), (12500, 128), jnp.float32)
        tbl_4 = 0.05 * jax.random.normal(jax.random.fold_in(_tk, 500 + 4), (1000, 128), jnp.float32)
        tbl_5 = 0.05 * jax.random.normal(jax.random.fold_in(_tk, 500 + 5), (12500, 128), jnp.float32)
        tbl_6 = 0.05 * jax.random.normal(jax.random.fold_in(_tk, 500 + 6), (1250, 128), jnp.float32)
        tbl_7 = 0.05 * jax.random.normal(jax.random.fold_in(_tk, 500 + 7), (1250, 128), jnp.float32)
        tbl_8 = 0.05 * jax.random.normal(jax.random.fold_in(_tk, 500 + 8), (1000, 128), jnp.float32)
        tbl_9 = 0.05 * jax.random.normal(jax.random.fold_in(_tk, 500 + 9), (1250, 128), jnp.float32)
        tbl_10 = 0.05 * jax.random.normal(jax.random.fold_in(_tk, 500 + 10), (1000, 128), jnp.float32)
        tbl_11 = 0.05 * jax.random.normal(jax.random.fold_in(_tk, 500 + 11), (12500, 128), jnp.float32)
        tbl_12 = 0.05 * jax.random.normal(jax.random.fold_in(_tk, 500 + 12), (1000, 128), jnp.float32)
        tbl_13 = 0.05 * jax.random.normal(jax.random.fold_in(_tk, 500 + 13), (1000, 128), jnp.float32)
        tbl_14 = 0.05 * jax.random.normal(jax.random.fold_in(_tk, 500 + 14), (1250, 128), jnp.float32)
        tbl_15 = 0.05 * jax.random.normal(jax.random.fold_in(_tk, 500 + 15), (12500, 128), jnp.float32)
        tbl_16 = 0.05 * jax.random.normal(jax.random.fold_in(_tk, 500 + 16), (1250, 128), jnp.float32)
        tbl_17 = 0.05 * jax.random.normal(jax.random.fold_in(_tk, 500 + 17), (12500, 128), jnp.float32)
        tbl_18 = 0.05 * jax.random.normal(jax.random.fold_in(_tk, 500 + 18), (1250, 128), jnp.float32)
        tbl_19 = 0.05 * jax.random.normal(jax.random.fold_in(_tk, 500 + 19), (1250, 128), jnp.float32)
        tbl_20 = 0.05 * jax.random.normal(jax.random.fold_in(_tk, 500 + 20), (12500, 128), jnp.float32)
        tbl_21 = 0.05 * jax.random.normal(jax.random.fold_in(_tk, 500 + 21), (1000, 128), jnp.float32)
        tbl_22 = 0.05 * jax.random.normal(jax.random.fold_in(_tk, 500 + 22), (12500, 128), jnp.float32)
        tbl_23 = 0.05 * jax.random.normal(jax.random.fold_in(_tk, 500 + 23), (1250, 128), jnp.float32)
        tbl_24 = 0.05 * jax.random.normal(jax.random.fold_in(_tk, 500 + 24), (1250, 128), jnp.float32)
        tbl_25 = 0.05 * jax.random.normal(jax.random.fold_in(_tk, 500 + 25), (1000, 128), jnp.float32)
        _rk = jax.random.fold_in(_tk, 7)
        r_dense_proj = -0.000520686 + 1.00062 * jax.random.normal(jax.random.fold_in(_rk, 101), (2048, 128), jnp.float32)
        W_top1 = 0.0405887 * jax.random.normal(jax.random.fold_in(_tk, 801), (607, 512), jnp.float32)
        W_top2 = 0.0441942 * jax.random.normal(jax.random.fold_in(_tk, 802), (512, 256), jnp.float32)
        W_top3 = 0.0625 * jax.random.normal(jax.random.fold_in(_tk, 803), (256, 1), jnp.float32)
        b_top1 = jnp.zeros((512,), jnp.float32)
        b_top2 = jnp.zeros((256,), jnp.float32)
        return (r_dense_proj, ids, tbl_0, tbl_1, tbl_2, tbl_3, tbl_4, tbl_5, tbl_6, tbl_7, tbl_8, tbl_9, tbl_10, tbl_11, tbl_12, tbl_13, tbl_14, tbl_15, tbl_16, tbl_17, tbl_18, tbl_19, tbl_20, tbl_21, tbl_22, tbl_23, tbl_24, tbl_25, W_top1, b_top1, W_top2, b_top2, W_top3)
    r_dense_proj, ids, tbl_0, tbl_1, tbl_2, tbl_3, tbl_4, tbl_5, tbl_6, tbl_7, tbl_8, tbl_9, tbl_10, tbl_11, tbl_12, tbl_13, tbl_14, tbl_15, tbl_16, tbl_17, tbl_18, tbl_19, tbl_20, tbl_21, tbl_22, tbl_23, tbl_24, tbl_25, W_top1, b_top1, W_top2, b_top2, W_top3 = _rec_inputs()

    def _L0_rec_setup():
        import jax, jax.numpy as jnp
        import numpy as np
        key = jax.random.key(seed)
        k1, k2 = jax.random.split(key)
        B, N_SPARSE, D = (2048, 26, 128)
        dense_proj = jax.random.normal(k1, (B, D), dtype=jnp.float32)
        sparse_embs = jax.random.normal(k2, (B, N_SPARSE, D), dtype=jnp.float32)
        return {'dense_proj': dense_proj, 'sparse_embs': sparse_embs}
    _L0_rec_all = _L0_rec_setup()
    _L0_rec_in = {k: v for k, v in _L0_rec_all.items() if k in ()}
    del _L0_rec_all
    return {'r_dense_proj': r_dense_proj, 'ids': ids, 'tbl_0': tbl_0, 'tbl_1': tbl_1, 'tbl_2': tbl_2, 'tbl_3': tbl_3, 'tbl_4': tbl_4, 'tbl_5': tbl_5, 'tbl_6': tbl_6, 'tbl_7': tbl_7, 'tbl_8': tbl_8, 'tbl_9': tbl_9, 'tbl_10': tbl_10, 'tbl_11': tbl_11, 'tbl_12': tbl_12, 'tbl_13': tbl_13, 'tbl_14': tbl_14, 'tbl_15': tbl_15, 'tbl_16': tbl_16, 'tbl_17': tbl_17, 'tbl_18': tbl_18, 'tbl_19': tbl_19, 'tbl_20': tbl_20, 'tbl_21': tbl_21, 'tbl_22': tbl_22, 'tbl_23': tbl_23, 'tbl_24': tbl_24, 'tbl_25': tbl_25, 'W_top1': W_top1, 'b_top1': b_top1, 'W_top2': W_top2, 'b_top2': b_top2, 'W_top3': W_top3}

def reference(r_dense_proj, ids, tbl_0, tbl_1, tbl_2, tbl_3, tbl_4, tbl_5, tbl_6, tbl_7, tbl_8, tbl_9, tbl_10, tbl_11, tbl_12, tbl_13, tbl_14, tbl_15, tbl_16, tbl_17, tbl_18, tbl_19, tbl_20, tbl_21, tbl_22, tbl_23, tbl_24, tbl_25, W_top1, b_top1, W_top2, b_top2, W_top3):
    import jax
    import jax.numpy as jnp

    def _L0_rec_ref(dense_proj, sparse_embs):
        import jax, jax.numpy as jnp
        import numpy as np
        all_vecs = jnp.concatenate([dense_proj[:, None, :], sparse_embs], axis=1)
        n = all_vecs.shape[1]
        interactions = jnp.einsum('bnd,bmd->bnm', all_vecs, all_vecs)
        rows, cols = np.triu_indices(n, k=1)
        interact_flat = interactions[:, rows, cols]
        return jnp.concatenate([dense_proj, interact_flat], axis=1)
    e = jnp.stack([tbl_0[ids[:, 0]], tbl_1[ids[:, 1]], tbl_2[ids[:, 2]], tbl_3[ids[:, 3]], tbl_4[ids[:, 4]], tbl_5[ids[:, 5]], tbl_6[ids[:, 6]], tbl_7[ids[:, 7]], tbl_8[ids[:, 8]], tbl_9[ids[:, 9]], tbl_10[ids[:, 10]], tbl_11[ids[:, 11]], tbl_12[ids[:, 12]], tbl_13[ids[:, 13]], tbl_14[ids[:, 14]], tbl_15[ids[:, 15]], tbl_16[ids[:, 16]], tbl_17[ids[:, 17]], tbl_18[ids[:, 18]], tbl_19[ids[:, 19]], tbl_20[ids[:, 20]], tbl_21[ids[:, 21]], tbl_22[ids[:, 22]], tbl_23[ids[:, 23]], tbl_24[ids[:, 24]], tbl_25[ids[:, 25]]], axis=1)
    z = _L0_rec_ref(r_dense_proj, e)
    z = z.reshape(z.shape[0], -1)
    h = jnp.concatenate([z, r_dense_proj], axis=1)
    h = jnp.maximum(h @ W_top1 + b_top1, 0.0)
    h = jnp.maximum(h @ W_top2 + b_top2, 0.0)
    y = h @ W_top3
    return y

_drawn_inputs = setup_inputs


def setup_inputs(seed=0):
    import zlib

    import numpy as np

    out = dict(_drawn_inputs(seed))
    spreads = {'b_top1': (0.0, 0.1), 'b_top2': (0.0, 0.1)}
    factors = {}
    for name, (base, spread) in spreads.items():
        noise = np.random.default_rng([zlib.crc32(name.encode()), seed]).standard_normal(out[name].shape)
        drawn = base * np.exp(spread * noise) if base else spread * noise
        out[name] = jnp.asarray(drawn.astype(out[name].dtype))
    for name, factor in factors.items():
        out[name] = (out[name] * factor).astype(out[name].dtype)
    return out
```

```python
import concourse.bass as bass
from concourse import mybir
from contextlib import ExitStack
import numpy as np

N_TABLES = 26


def triangle_rows(first_row):
    n_vec = N_TABLES + 1
    rows, cols = np.triu_indices(n_vec, k=1)
    place = np.zeros((n_vec, n_vec), dtype=np.int64)
    place[rows, cols] = np.arange(len(rows))
    place[cols, rows] = np.arange(len(rows))
    return np.array([first_row + place[n, (n + k) % n_vec] for n in range(n_vec) for k in range(1, n_vec // 2 + 1)])


def dlrm_tower(nc, dense, ids, tables, w1_dense, w1_pairs, w1_again, b1, w2, b2, w3, y):
    fp32 = mybir.dt.float32
    ALU = mybir.AluOpType
    ACT = mybir.ActivationFunctionType

    P = 128
    B, D = dense.shape
    NT = ids.shape[1]
    NV = NT + 1
    NP_ = 32
    KD = NV // 2
    NC = 3
    VC = NV // NC
    KP = VC * KD
    Q = 32
    NQ = P // Q
    TILES = B // P
    U = 2
    TURNS = TILES // U
    UB = U * P
    G4 = 4
    NG = -(-NV // G4)
    H1 = w1_dense.shape[1]
    H2 = w2.shape[1]
    C1, C2 = H1 // P, H2 // P
    groups = [list(range(g * G4, min(NV, (g + 1) * G4))) for g in range(NG)]

    ctx = ExitStack()
    with ctx:
        def sb(name, shape, dt=fp32):
            return ctx.enter_context(nc.sbuf_tensor(name, shape, dt))

        def pb(name, shape):
            return ctx.enter_context(nc.psum_tensor(name, shape, fp32))

        def sem(name):
            return ctx.enter_context(nc.semaphore(name))

        index = [sb(f"index{u}", [P, NT], mybir.dt.int32) for u in range(U)]
        rows = [sb(f"rows{u}", [P, NV * D]) for u in range(U)]
        vecs = [sb(f"vecs{u}", [D, P, NV]) for u in range(U)]
        gram_b = [sb(f"gram_b{u}", [P, (NV + KD) * NP_]) for u in range(U)]
        pairs_b = [sb(f"pairs_b{u}", [P, NV * KD]) for u in range(U)]
        pairs_t = sb("pairs_t", [KP, NC, UB])
        dense_t = sb("dense_t", [D, UB])
        h1_t = sb("h1_t", [P, C1, UB])
        h2_t = sb("h2_t", [P, C2, UB])
        y_row = sb("y_row", [1, UB])
        ident = sb("ident", [P, P])
        w1d = sb("w1d", [D, H1])
        w1e = sb("w1e", [D, H1])
        w1s = sb("w1s", [D, H1])
        w1p = sb("w1p", [KP, NC, H1])
        w2s = sb("w2s", [P, C1, H2])
        w3s = sb("w3s", [P, C2])
        b1s = sb("b1s", [P, C1])
        b2s = sb("b2s", [P, C2])

        vec_ps = [pb(f"vec_ps{i}", [P, 512]) for i in range(2)]
        gram_ps = pb("gram_ps", [P, Q * NP_])
        pair_ps = pb("pair_ps", [P, 512])
        h1_ps = pb("h1_ps", [P, C1, UB])
        h2_ps = pb("h2_ps", [P, C2, UB])

        index_in = [sem(f"index_in{u}") for u in range(U)]
        dense_in = [sem(f"dense_in{u}") for u in range(U)]
        gathered = [[sem(f"gathered{u}_{g}") for g in range(NG)] for u in range(U)]
        tiles_begun = sem("tiles_begun")
        weights_in = sem("weights_in")
        ident_zero = sem("ident_zero")
        ident_ready = sem("ident_ready")
        w1_summed = sem("w1_summed")
        gram_cleared = sem("gram_cleared")
        vec_made = sem("vec_made")
        vec_kept = sem("vec_kept")
        gram_made = sem("gram_made")
        gram_kept = sem("gram_kept")
        pairs_picked = sem("pairs_picked")
        pairs_made = sem("pairs_made")
        pairs_kept = sem("pairs_kept")
        dense_kept = sem("dense_kept")
        h1_made = sem("h1_made")
        h1_kept = sem("h1_kept")
        h2_made = sem("h2_made")
        h2_kept = sem("h2_kept")
        y_made = sem("y_made")
        y_kept = sem("y_kept")
        y_out = sem("y_out")

        block = ctx.enter_context(nc.Block())

        ids_t = ids.rearrange("(t p) f -> t p f", p=P)
        dense_rows = dense.rearrange("(t p) d -> t p d", p=P)
        y_rows = y.rearrange("(t b) o -> t o b", b=UB)

        @block.sync
        def _(sp):
            for u in range(U):
                sp.dma_start(index[u][:, :], ids_t[u, :, :]).then_inc(index_in[u], 16)
            for u in range(U):
                sp.dma_start(rows[u][:, 0:D], dense_rows[u, :, :]).then_inc(dense_in[u], 16)
            sp.dma_start(w1d[:, :], w1_dense[:, :]).then_inc(weights_in, 16)
            sp.dma_start(w1e[:, :], w1_again[:, :]).then_inc(weights_in, 16)
            sp.dma_start(w1p[:, :, :], w1_pairs.rearrange("(c k) n -> k c n", k=KP)).then_inc(weights_in, 16)
            sp.dma_start(w2s[:, :, :], w2.rearrange("(c k) n -> k c n", k=P)).then_inc(weights_in, 16)
            with nc.allow_non_contiguous_dma(reason="small columns, once"):
                sp.dma_start(w3s[:, :], w3.rearrange("(c k) o -> k (c o)", k=P)).then_inc(weights_in, 16)
                sp.dma_start(b1s[:, :], b1.rearrange("(c k) -> k c", k=P)).then_inc(weights_in, 16)
                sp.dma_start(b2s[:, :], b2.rearrange("(c k) -> k c", k=P)).then_inc(weights_in, 16)
            with sp.Fori(1, TURNS) as i:
                for u in range(U):
                    sp.wait_ge(vec_made, (i * U + (u - U + 1)) * NG)
                    sp.dma_start(index[u][:, :], ids_t[i * U + u, :, :]).then_inc(index_in[u], 16)
                    sp.dma_start(rows[u][:, 0:D], dense_rows[i * U + u, :, :]).then_inc(dense_in[u], 16)

        @block.gpsimd
        def _(pool):
            nc.gpsimd.memset(ident[:, :], 0.0).then_inc(ident_zero, 1)
            pool.wait_ge(ident_zero, 1)
            nc.gpsimd.affine_select(out=ident[:, :], in_=ident[:, :], compare_op=ALU.not_equal, fill=1.0, base=0,
                                    pattern=[[-1, P]], channel_multiplier=1).then_inc(ident_ready, 1)

            def gather_tile(turn, u, first):
                if not first:
                    pool.wait_ge(vec_made, (turn * U + (u - U + 1)) * NG)
                pool.wait_ge(index_in[u], (turn + 1) * 16)
                pool.sem_inc(tiles_begun, 1)
                for g in range(NG):
                    for v in groups[g]:
                        if v == 0:
                            continue
                        nc.gpsimd.indirect_dma_start(
                            out=rows[u][:, v * D:(v + 1) * D], out_offset=None, in_=tables[v - 1][:, :],
                            in_offset=bass.IndirectOffsetOnAxis(ap=index[u][:, v - 1:v], axis=0),
                        ).then_inc(gathered[u][g], 16)

            for u in range(U):
                gather_tile(0, u, True)
            with pool.Fori(1, TURNS) as i:
                for u in range(U):
                    gather_tile(i, u, False)

        @block.tensor
        def _(pe):
            def tile_vectors(turn, u, first):
                for g in range(NG):
                    if g == 0:
                        pe.wait_ge(dense_in[u], (turn + 1) * 16)
                    pe.wait_ge(gathered[u][g], (turn + 1) * (16 * len([v for v in groups[g] if v > 0])))
                    at = u * NG + g
                    if not (first and at < 2):
                        pe.wait_ge(vec_kept, turn * (U * NG) + (at - 1))
                    for k, v in enumerate(groups[g]):
                        last = nc.tensor.transpose(vec_ps[at % 2][:, k * P:(k + 1) * P], rows[u][:, v * D:(v + 1) * D],
                                                   ident[:, :])
                    last.then_inc(vec_made, 1)

            def tile_gram(turn, u, first):
                pe.wait_ge(vec_kept, turn * (U * NG) + (u + 1) * NG)
                if not (first and u == 0):
                    pe.wait_ge(gram_kept, turn * U + u)
                for j in range(Q):
                    for q in range(NQ):
                        mine = vecs[u][:, q * Q + j, :]
                        last = nc.tensor.matmul(gram_ps[q * Q:q * Q + NV, j * NP_:j * NP_ + NV], mine, mine,
                                                start=True, stop=True)
                last.then_inc(gram_made, 1)

            def tile_pairs(turn, u, first):
                pe.wait_ge(pairs_picked, turn * U + (u + 1))
                if not (first and u == 0):
                    pe.wait_ge(pairs_kept, turn * U + u)
                for c in range(NC):
                    last = nc.tensor.transpose(pair_ps[0:KP, c * P:(c + 1) * P], pairs_b[u][:, c * KP:(c + 1) * KP],
                                               ident[:, :])
                last.then_inc(pairs_made, 1)

            def turn_mlp(turn, first):
                pe.wait_ge(pairs_kept, turn * U + U)
                pe.wait_ge(dense_kept, turn * U + U)
                if not first:
                    pe.wait_ge(h1_kept, turn * C1)
                for o in range(C1):
                    cols = slice(o * P, (o + 1) * P)
                    nc.tensor.matmul(h1_ps[:, o, :], w1s[:, cols], dense_t[:, :], start=True, stop=False)
                    for c in range(NC):
                        last = nc.tensor.matmul(h1_ps[:, o, :], w1p[:, c, cols], pairs_t[:, c, :], start=False,
                                                stop=c == NC - 1)
                    last.then_inc(h1_made, 1)
                if not first:
                    pe.wait_ge(y_kept, turn)
                pe.wait_ge(h1_kept, (turn + 1) * C1)
                for o in range(C2):
                    for c in range(C1):
                        last = nc.tensor.matmul(h2_ps[:, o, :], w2s[:, c, o * P:(o + 1) * P], h1_t[:, c, :],
                                                start=c == 0, stop=c == C1 - 1)
                    last.then_inc(h2_made, 1)
                pe.wait_ge(h2_kept, (turn + 1) * C2)
                for c in range(C2):
                    last = nc.tensor.matmul(h2_ps[0:1, 0, :], w3s[:, c:c + 1], h2_t[:, c, :], start=c == 0,
                                            stop=c == C2 - 1)
                last.then_inc(y_made, 1)

            def turn_all(turn, first):
                for u in range(U):
                    tile_vectors(turn, u, first)
                    tile_gram(turn, u, first)
                    tile_pairs(turn, u, first)
                turn_mlp(turn, first)

            pe.wait_ge(ident_ready, 1)
            pe.wait_ge(gram_cleared, 1)
            pe.wait_ge(w1_summed, 1)
            turn_all(0, True)
            with pe.Fori(1, TURNS) as i:
                turn_all(i, False)

        @block.scalar
        def _(act):
            def turn_all(turn, first):
                for u in range(U):
                    for g in range(NG):
                        at = u * NG + g
                        n = len(groups[g])
                        act.wait_ge(vec_made, turn * (U * NG) + (at + 1))
                        if g == 0 and not first:
                            act.wait_ge(gram_made, turn * U + (u - U + 1))
                        src = vec_ps[at % 2][:, 0:n * P].rearrange("p (v b) -> p b v", b=P)
                        if g == 0:
                            if u == 0 and not first:
                                act.wait_ge(h1_made, turn * C1)
                            nc.scalar.copy(dense_t[:, u * P:(u + 1) * P], vec_ps[at % 2][:, 0:P]).then_inc(dense_kept, 1)
                        nc.scalar.copy(vecs[u][:, :, g * G4:g * G4 + n], src).then_inc(vec_kept, 1)
                    act.wait_ge(pairs_made, turn * U + (u + 1))
                    nc.scalar.copy(pairs_t[:, :, u * P:(u + 1) * P],
                                   pair_ps[0:KP, 0:NC * P].rearrange("p (c b) -> p c b", b=P)).then_inc(pairs_kept, 1)
                if not first:
                    act.wait_ge(h2_made, turn * C2)
                for o in range(C1):
                    act.wait_ge(h1_made, turn * C1 + (o // 2 * 2 + 2))
                    nc.scalar.activation(h1_t[:, o, :], h1_ps[:, o, :], ACT.Relu, bias=b1s[:, o:o + 1]).then_inc(h1_kept, 1)
                if not first:
                    act.wait_ge(y_made, turn)
                for o in range(C2):
                    act.wait_ge(h2_made, turn * C2 + C2)
                    nc.scalar.activation(h2_t[:, o, :], h2_ps[:, o, :], ACT.Relu, bias=b2s[:, o:o + 1]).then_inc(h2_kept, 1)
                act.wait_ge(y_made, turn + 1)
                if not first:
                    act.wait_ge(y_out, turn * 16)
                nc.scalar.copy(y_row[:, :], h2_ps[0:1, 0, :]).then_inc(y_kept, 1)
                act.wait_ge(y_kept, turn + 1)
                act.dma_start(y_rows[turn, :, :], y_row[:, :]).then_inc(y_out, 16)

            act.wait_ge(weights_in, 7 * 16)
            turn_all(0, True)
            with act.Fori(1, TURNS) as i:
                turn_all(i, False)
            act.wait_ge(y_out, TURNS * 16)

        @block.vector
        def _(dve):
            nc.vector.memset(gram_ps[:, :], 0.0).then_inc(gram_cleared, 1)
            dve.wait_ge(weights_in, 7 * 16)
            nc.vector.tensor_tensor(w1s[:, :], w1d[:, :], w1e[:, :], ALU.add).then_inc(w1_summed, 1)

            def turn_all(turn, first):
                for u in range(U):
                    dve.wait_ge(gram_made, turn * U + (u + 1))
                    if not first:
                        dve.wait_ge(pairs_made, turn * U + (u - U + 1))
                    src = gram_ps[:, :].rearrange("p (j m) -> p m j", m=NP_)
                    nc.vector.transpose(gram_b[u][:, 0:NV * NP_], src[:, 0:NV, :])
                    nc.vector.transpose(gram_b[u][:, NV * NP_:], src[:, 0:KD, :]).then_inc(gram_kept, 1)
                    dve.wait_ge(gram_kept, turn * U + (u + 1))
                    picked = bass.AP(gram_b[u], NP_, [[(NV + KD) * NP_, P], [NP_ + 1, NV], [NP_, KD]])
                    nc.vector.tensor_copy(pairs_b[u][:, :].rearrange("p (n k) -> p n k", k=KD),
                                          picked).then_inc(pairs_picked, 1)

            turn_all(0, True)
            with dve.Fori(1, TURNS) as i:
                turn_all(i, False)


def kernel(r_dense_proj, ids, W_top1, b_top1, W_top2, b_top2, W_top3, **tables):
    import concourse.bacc as bacc
    from concourse.bass_utils import run_bass_kernel_spmd

    nc = bacc.Bacc("TRN2", target_bir_lowering=False, num_devices=1)
    arrays = {}

    def given(name, a):
        a = np.ascontiguousarray(a)
        arrays[name] = a
        return nc.dram_tensor(name, a.shape, mybir.dt.from_np(a.dtype), kind="ExternalInput").ap()

    D = r_dense_proj.shape[1]
    W = np.asarray(W_top1)
    args = [
        given("dense", r_dense_proj), given("ids", ids),
        [given(f"tbl_{f}", tables[f"tbl_{f}"]) for f in range(N_TABLES)],
        given("w1_dense", W[0:D]), given("w1_pairs", W[triangle_rows(D)]), given("w1_again", W[W.shape[0] - D:]),
        given("b1", b_top1), given("w2", W_top2), given("b2", b_top2), given("w3", W_top3),
    ]
    y = nc.dram_tensor("y", (r_dense_proj.shape[0], W_top3.shape[1]), mybir.dt.float32, kind="ExternalOutput").ap()
    dlrm_tower(nc, *args, y)
    r = run_bass_kernel_spmd(nc, [arrays], core_ids=[0])
    return r.results[0]["y"]
```

```python
import concourse.bass as bass
from concourse import mybir
from contextlib import ExitStack
import numpy as np

N_TABLES = 26
N_MATRIX = 7


def lookup_order(sizes):
    smallest = sorted(range(len(sizes)), key=lambda f: (sizes[f], f))[:N_MATRIX]
    return [f for f in range(len(sizes)) if f not in smallest] + sorted(smallest)


def pair_rows(first_row, order):
    vector = [0] + [1 + f for f in order]
    n_vec = len(vector)
    rows, cols = np.triu_indices(n_vec, k=1)
    place = np.zeros((n_vec, n_vec), dtype=np.int64)
    place[rows, cols] = np.arange(len(rows))
    place[cols, rows] = np.arange(len(rows))
    return np.array([first_row + place[vector[n], vector[(n + k) % n_vec]]
                     for n in range(n_vec) for k in range(1, n_vec // 2 + 1)])


def dlrm_tower(nc, dense, ids_gather, ids_matrix, gather_tables, matrix_tables,
               w1_dense, w1_pairs, w1_again, b1, w2, b2, w3, y):
    fp32 = mybir.dt.float32
    fp32r = mybir.dt.float32r
    ALU = mybir.AluOpType
    ACT = mybir.ActivationFunctionType

    P = 128
    B, D = dense.shape
    NGT = len(gather_tables)
    NMT = len(matrix_tables)
    NT_ = 1 + NGT
    NV = NT_ + NMT
    PITCH = 32
    KD = NV // 2
    NC = 3
    KP = NV * KD // NC
    Q = 32
    NQ = P // Q
    U = 2
    UB = U * P
    TURNS = B // UB
    G4 = 4
    NG = NT_ // G4
    MG = -(-NMT // 2)
    V = matrix_tables[0].shape[0]
    KV = 125
    CV = V // KV
    EARLY = 2
    H1 = w1_dense.shape[1]
    H2 = w2.shape[1]
    C1, C2 = H1 // P, H2 // P
    assert NT_ % G4 == 0 and V % KV == 0 and (MG + U * NG) % 2 == 0
    assert all(t.shape[0] == V for t in matrix_tables)
    groups = [list(range(g * G4, (g + 1) * G4)) for g in range(NG)]
    gathers = [len([v for v in g if v > 0]) for g in groups]

    ctx = ExitStack()
    with ctx:
        def sb(name, shape, dt=fp32):
            return ctx.enter_context(nc.sbuf_tensor(name, shape, dt))

        def pb(name, shape):
            return ctx.enter_context(nc.psum_tensor(name, shape, fp32))

        def sem(name):
            return ctx.enter_context(nc.semaphore(name))

        index = [sb(f"index{u}", [P, NGT], mybir.dt.int32) for u in range(U)]
        rows = [sb(f"rows{u}", [P, NT_ * D]) for u in range(U)]
        vecs = [sb(f"vecs{u}", [D, P, NV]) for u in range(U)]
        ids_early = sb("ids_early", [KV, EARLY, UB], mybir.dt.int32)
        ids_late = sb("ids_late", [KV, NMT - EARLY, UB], mybir.dt.int32)
        row_no = sb("row_no", [KV, CV], mybir.dt.int32)
        row_nof = sb("row_nof", [KV, CV])
        select = [sb(f"select{i}", [KV, CV, UB], fp32r) for i in range(2)]
        table_raw = [sb(f"table_raw{i}", [KV, CV, D]) for i in range(2)]
        table_hi = sb("table_hi", [KV, NMT, CV, D], fp32r)
        table_lo = sb("table_lo", [KV, NMT, CV, D], fp32r)
        gram_b = [sb(f"gram_b{u}", [P, (NV + KD) * PITCH]) for u in range(U)]
        pairs_b = [sb(f"pairs_b{u}", [P, NV * KD]) for u in range(U)]
        pairs_t = sb("pairs_t", [KP, NC, UB])
        dense_t = sb("dense_t", [D, UB])
        h1_t = sb("h1_t", [P, C1, UB])
        h2_t = sb("h2_t", [P, C2, UB])
        y_row = sb("y_row", [1, UB])
        ident = sb("ident", [P, P])
        w1d = sb("w1d", [D, H1])
        w1e = sb("w1e", [D, H1])
        w1s = sb("w1s", [D, H1])
        w1p = sb("w1p", [KP, NC, H1])
        w2s = sb("w2s", [P, C1, H2])
        w3s = sb("w3s", [P, C2])
        b1s = sb("b1s", [P, C1])
        b2s = sb("b2s", [P, C2])

        vec_ps = [pb(f"vec_ps{i}", [P, 512]) for i in range(2)]
        gram_ps = pb("gram_ps", [P, Q * PITCH])
        pair_ps = pb("pair_ps", [P, 512])
        h1_ps = pb("h1_ps", [P, C1, UB])
        h2_ps = pb("h2_ps", [P, C2, UB])

        index_in = [sem(f"index_in{u}") for u in range(U)]
        dense_in = [sem(f"dense_in{u}") for u in range(U)]
        early_in = sem("early_in")
        late_in = sem("late_in")
        table_in = [sem(f"table_in{i}") for i in range(2)]
        gathered = [[sem(f"gathered{u}_{g}") for g in range(NG)] for u in range(U)]
        tiles_begun = sem("tiles_begun")
        weights_in = sem("weights_in")
        ident_zero = sem("ident_zero")
        ident_ready = sem("ident_ready")
        row_no_made = sem("row_no_made")
        row_no_ready = sem("row_no_ready")
        hi_ready = sem("hi_ready")
        lo_ready = sem("lo_ready")
        w1_summed = sem("w1_summed")
        gram_cleared = sem("gram_cleared")
        selected = sem("selected")
        looked_up = sem("looked_up")
        looked_kept = sem("looked_kept")
        vec_made = sem("vec_made")
        kept_act = sem("kept_act")
        kept_dve = sem("kept_dve")
        gram_made = sem("gram_made")
        gram_kept = sem("gram_kept")
        pairs_picked = sem("pairs_picked")
        pairs_made = sem("pairs_made")
        pairs_kept = sem("pairs_kept")
        dense_kept = sem("dense_kept")
        h1_made = sem("h1_made")
        h1_kept = sem("h1_kept")
        h2_made = sem("h2_made")
        h2_kept = sem("h2_kept")
        y_made = sem("y_made")
        y_kept = sem("y_kept")
        y_out = sem("y_out")

        FILLS = MG + U * NG

        def fill_of(u, g):
            return MG + u * NG + g

        def by_act(u, g):
            return fill_of(u, g) % 2 == 0

        def groups_kept(engine_is_act, upto):
            return len([f for f in range(MG, upto + 1) if (f % 2 == 0) == engine_is_act])

        PER_ACT = groups_kept(True, FILLS - 1)
        PER_DVE = groups_kept(False, FILLS - 1)

        def wait_bank(pe, turn, fill, first):
            last = fill - 2
            if last < 0:
                if first:
                    return
                last += FILLS
                if last % 2 == 0:
                    pe.wait_ge(kept_act, turn * PER_ACT)
                else:
                    pe.wait_ge(kept_dve, turn * PER_DVE)
            elif last < MG:
                pe.wait_ge(looked_kept, turn * MG + (last + 1))
            elif last % 2 == 0:
                pe.wait_ge(kept_act, turn * PER_ACT + groups_kept(True, last))
            else:
                pe.wait_ge(kept_dve, turn * PER_DVE + groups_kept(False, last))

        block = ctx.enter_context(nc.Block())

        ids_g = ids_gather.rearrange("(t p) f -> t p f", p=P)
        dense_rows = dense.rearrange("(t p) d -> t p d", p=P)
        y_rows = y.rearrange("(t b) o -> t o b", b=UB)
        ids_m = ids_matrix.rearrange("f (t b) -> t f b", b=UB)

        def on_all(turn, lo, hi):
            return ids_m[turn, lo:hi, :].rearrange("f (o b) -> o f b", o=1).broadcast_to([KV, hi - lo, UB])

        @block.sync
        def _(sp):
            for u in range(U):
                sp.dma_start(index[u][:, :], ids_g[u, :, :]).then_inc(index_in[u], 16)
            sp.dma_start(ids_early[:, :, :], on_all(0, 0, EARLY)).then_inc(early_in, 16)
            for m in range(NMT):
                if m >= 2:
                    sp.wait_ge(lo_ready, m - 1)
                sp.dma_start(table_raw[m % 2][:, :, :],
                             matrix_tables[m].rearrange("(c k) d -> k c d", k=KV)).then_inc(table_in[m % 2], 16)
                if m == 1:
                    sp.dma_start(ids_late[:, :, :], on_all(0, EARLY, NMT)).then_inc(late_in, 16)
                    for u in range(U):
                        sp.dma_start(rows[u][:, 0:D], dense_rows[u, :, :]).then_inc(dense_in[u], 16)
            with sp.Fori(1, TURNS) as i:
                sp.wait_ge(selected, (i - 1) * NMT + EARLY)
                sp.dma_start(ids_early[:, :, :], on_all(i, 0, EARLY)).then_inc(early_in, 16)
                sp.wait_ge(selected, i * NMT)
                sp.dma_start(ids_late[:, :, :], on_all(i, EARLY, NMT)).then_inc(late_in, 16)
                for u in range(U):
                    sp.wait_ge(vec_made, (i * U + (u - U + 1)) * NG)
                    sp.dma_start(index[u][:, :], ids_g[i * U + u, :, :]).then_inc(index_in[u], 16)
                    sp.dma_start(rows[u][:, 0:D], dense_rows[i * U + u, :, :]).then_inc(dense_in[u], 16)

        @block.gpsimd
        def _(pool):
            nc.gpsimd.iota(row_no[:, :], pattern=[[KV, CV]], base=0, channel_multiplier=1).then_inc(row_no_made, 1)
            nc.gpsimd.memset(ident[:, :], 0.0).then_inc(ident_zero, 1)
            pool.wait_ge(ident_zero, 1)
            nc.gpsimd.affine_select(out=ident[:, :], in_=ident[:, :], compare_op=ALU.not_equal, fill=1.0, base=0,
                                    pattern=[[-1, P]], channel_multiplier=1).then_inc(ident_ready, 1)

            def gather_tile(turn, u, first):
                if not first:
                    pool.wait_ge(vec_made, (turn * U + (u - U + 1)) * NG)
                pool.wait_ge(index_in[u], (turn + 1) * 16)
                pool.sem_inc(tiles_begun, 1)
                for g in range(NG):
                    for v in groups[g]:
                        if v > 0:
                            nc.gpsimd.indirect_dma_start(
                                out=rows[u][:, v * D:(v + 1) * D], out_offset=None, in_=gather_tables[v - 1][:, :],
                                in_offset=bass.IndirectOffsetOnAxis(ap=index[u][:, v - 1:v], axis=0),
                            ).then_inc(gathered[u][g], 16)

            for u in range(U):
                gather_tile(0, u, True)
            with pool.Fori(1, TURNS) as i:
                for u in range(U):
                    gather_tile(i, u, False)

        @block.tensor
        def _(pe):
            def look_up(turn, group, first):
                wait_bank(pe, turn, group, first)
                for m in range(2 * group, min(2 * group + 2, NMT)):
                    if first:
                        pe.wait_ge(hi_ready, m + 1)
                        pe.wait_ge(lo_ready, m + 1)
                    pe.wait_ge(selected, turn * NMT + (m + 1))
                    out = vec_ps[group % 2][:, (m % 2) * UB:(m % 2 + 1) * UB]
                    for c in range(CV):
                        for part in (table_hi, table_lo):
                            last = nc.tensor.matmul(out, part[:, m, c, :], select[m % 2][:, c, :],
                                                    start=c == 0 and part is table_hi,
                                                    stop=c == CV - 1 and part is table_lo)
                    last.then_inc(looked_up, 1)

            def tile_vectors(turn, u, first):
                for g in range(NG):
                    if g == 0:
                        pe.wait_ge(dense_in[u], (turn + 1) * 16)
                    pe.wait_ge(gathered[u][g], (turn + 1) * (16 * gathers[g]))
                    fill = fill_of(u, g)
                    wait_bank(pe, turn, fill, first)
                    for k, v in enumerate(groups[g]):
                        last = nc.tensor.transpose(vec_ps[fill % 2][:, k * P:(k + 1) * P],
                                                   rows[u][:, v * D:(v + 1) * D], ident[:, :])
                    last.then_inc(vec_made, 1)

            def tile_gram(turn, u, first):
                pe.wait_ge(kept_act, turn * PER_ACT + groups_kept(True, fill_of(u, NG - 1)))
                pe.wait_ge(kept_dve, turn * PER_DVE + groups_kept(False, fill_of(u, NG - 1)))
                pe.wait_ge(looked_kept, (turn + 1) * MG)
                if not (first and u == 0):
                    pe.wait_ge(gram_kept, turn * U + u)
                for j in range(Q):
                    for q in range(NQ):
                        mine = vecs[u][:, q * Q + j, :]
                        last = nc.tensor.matmul(gram_ps[q * Q:q * Q + NV, j * PITCH:j * PITCH + NV], mine, mine,
                                                start=True, stop=True)
                last.then_inc(gram_made, 1)

            def tile_pairs(turn, u, first):
                pe.wait_ge(pairs_picked, turn * U + (u + 1))
                if not (first and u == 0):
                    pe.wait_ge(pairs_kept, turn * U + u)
                for c in range(NC):
                    last = nc.tensor.transpose(pair_ps[0:KP, c * P:(c + 1) * P], pairs_b[u][:, c * KP:(c + 1) * KP],
                                               ident[:, :])
                last.then_inc(pairs_made, 1)

            def layer1(turn, first):
                pe.wait_ge(pairs_kept, turn * U + U)
                pe.wait_ge(dense_kept, turn * U + U)
                if not first:
                    pe.wait_ge(h1_kept, turn * C1)
                for o in range(C1):
                    cols = slice(o * P, (o + 1) * P)
                    nc.tensor.matmul(h1_ps[:, o, :], w1s[:, cols], dense_t[:, :], start=True, stop=False)
                    for c in range(NC):
                        last = nc.tensor.matmul(h1_ps[:, o, :], w1p[:, c, cols], pairs_t[:, c, :], start=False,
                                                stop=c == NC - 1)
                    last.then_inc(h1_made, 1)

            def layer2(turn, first):
                if not first:
                    pe.wait_ge(y_kept, turn)
                pe.wait_ge(h1_kept, (turn + 1) * C1)
                for o in range(C2):
                    for c in range(C1):
                        last = nc.tensor.matmul(h2_ps[:, o, :], w2s[:, c, o * P:(o + 1) * P], h1_t[:, c, :],
                                                start=c == 0, stop=c == C1 - 1)
                    last.then_inc(h2_made, 1)

            def layer3(turn):
                pe.wait_ge(h2_kept, (turn + 1) * C2)
                for c in range(C2):
                    last = nc.tensor.matmul(h2_ps[0:1, 0, :], w3s[:, c:c + 1], h2_t[:, c, :], start=c == 0,
                                            stop=c == C2 - 1)
                last.then_inc(y_made, 1)

            def turn_all(turn, before, first, second):
                for group in range(MG):
                    look_up(turn, group, first)
                    if group == 0 and not first:
                        tile_pairs(before, U - 1, False)
                if not first:
                    layer1(before, second)
                tile_vectors(turn, 0, first)
                if not first:
                    layer2(before, second)
                tile_gram(turn, 0, first)
                tile_vectors(turn, 1, first)
                tile_pairs(turn, 0, first)
                if not first:
                    layer3(before)
                tile_gram(turn, 1, first)

            pe.wait_ge(ident_ready, 1)
            pe.wait_ge(gram_cleared, 1)
            turn_all(0, None, True, False)
            pe.wait_ge(w1_summed, 1)
            turn_all(1, 0, False, True)
            with pe.Fori(2, TURNS) as i:
                turn_all(i, i - 1, False, False)
            tile_pairs(TURNS - 1, U - 1, False)
            layer1(TURNS - 1, False)
            layer2(TURNS - 1, False)
            layer3(TURNS - 1)

        @block.scalar
        def _(act):
            act.dma_start(w1d[:, :], w1_dense[:, :]).then_inc(weights_in, 16)
            act.dma_start(w1e[:, :], w1_again[:, :]).then_inc(weights_in, 16)
            act.dma_start(w1p[:, :, :], w1_pairs.rearrange("(c k) n -> k c n", k=KP)).then_inc(weights_in, 16)
            act.dma_start(w2s[:, :, :], w2.rearrange("(c k) n -> k c n", k=P)).then_inc(weights_in, 16)
            with nc.allow_non_contiguous_dma(reason="small columns, once"):
                act.dma_start(w3s[:, :], w3.rearrange("(c k) o -> k (c o)", k=P)).then_inc(weights_in, 16)
                act.dma_start(b1s[:, :], b1.rearrange("(c k) -> k c", k=P)).then_inc(weights_in, 16)
                act.dma_start(b2s[:, :], b2.rearrange("(c k) -> k c", k=P)).then_inc(weights_in, 16)
            for m in range(NMT):
                act.wait_ge(table_in[m % 2], (m // 2 + 1) * 16)
                nc.scalar.copy(table_hi[:, m, :, :], table_raw[m % 2][:, :, :]).then_inc(hi_ready, 1)

            def keep_looked_up(turn, group, first):
                n = min(2, NMT - 2 * group)
                act.wait_ge(looked_up, turn * NMT + (2 * group + n))
                if group == 0 and not first:
                    act.wait_ge(gram_made, turn * U)
                at = NT_ + 2 * group
                for u in range(U):
                    src = vec_ps[group % 2][:, 0:n * UB].rearrange("p (m u b) -> p u b m", u=U, b=P)
                    last = nc.scalar.copy(vecs[u][:, :, at:at + n], src[:, u])
                last.then_inc(looked_kept, 1)

            def keep_pairs(turn, u):
                act.wait_ge(pairs_made, turn * U + (u + 1))
                nc.scalar.copy(pairs_t[:, :, u * P:(u + 1) * P],
                               pair_ps[0:KP, 0:NC * P].rearrange("p (c b) -> p c b", b=P)).then_inc(pairs_kept, 1)

            def keep_vectors(turn, u):
                for g in range(NG):
                    bank = vec_ps[fill_of(u, g) % 2]
                    if not by_act(u, g):
                        continue
                    act.wait_ge(vec_made, turn * (U * NG) + (u * NG + g + 1))
                    nc.scalar.copy(vecs[u][:, :, g * G4:(g + 1) * G4],
                                   bank[:, :].rearrange("p (v b) -> p b v", b=P)).then_inc(kept_act, 1)
                act.wait_ge(kept_act, turn * PER_ACT + groups_kept(True, fill_of(u, NG - 1)))
                act.wait_ge(kept_dve, turn * PER_DVE + groups_kept(False, fill_of(u, NG - 1)))
                nc.scalar.copy(dense_t[:, u * P:(u + 1) * P], vecs[u][:, :, 0]).then_inc(dense_kept, 1)

            def relu1(turn, first):
                if not first:
                    act.wait_ge(h2_made, turn * C2)
                for o in range(C1):
                    act.wait_ge(h1_made, turn * C1 + (o // 2 * 2 + 2))
                    nc.scalar.activation(h1_t[:, o, :], h1_ps[:, o, :], ACT.Relu, bias=b1s[:, o:o + 1]).then_inc(h1_kept, 1)

            def relu2(turn, first):
                if not first:
                    act.wait_ge(y_made, turn)
                act.wait_ge(h2_made, turn * C2 + C2)
                for o in range(C2):
                    nc.scalar.activation(h2_t[:, o, :], h2_ps[:, o, :], ACT.Relu, bias=b2s[:, o:o + 1]).then_inc(h2_kept, 1)

            def give_y(turn, first):
                act.wait_ge(y_made, turn + 1)
                if not first:
                    act.wait_ge(y_out, turn * 16)
                nc.scalar.copy(y_row[:, :], h2_ps[0:1, 0, :]).then_inc(y_kept, 1)
                act.wait_ge(y_kept, turn + 1)
                act.dma_start(y_rows[turn, :, :], y_row[:, :]).then_inc(y_out, 16)

            def turn_all(turn, before, first, second):
                for group in range(MG):
                    keep_looked_up(turn, group, first)
                    if group == 0 and not first:
                        keep_pairs(before, U - 1)
                if not first:
                    relu1(before, second)
                keep_vectors(turn, 0)
                if not first:
                    relu2(before, second)
                keep_vectors(turn, 1)
                keep_pairs(turn, 0)
                if not first:
                    give_y(before, second)

            turn_all(0, None, True, False)
            act.wait_ge(weights_in, 7 * 16)
            turn_all(1, 0, False, True)
            with act.Fori(2, TURNS) as i:
                turn_all(i, i - 1, False, False)
            keep_pairs(TURNS - 1, U - 1)
            relu1(TURNS - 1, False)
            relu2(TURNS - 1, False)
            give_y(TURNS - 1, False)
            act.wait_ge(y_out, TURNS * 16)

        @block.vector
        def _(dve):
            nc.vector.memset(gram_ps[:, :], 0.0).then_inc(gram_cleared, 1)
            dve.wait_ge(row_no_made, 1)
            nc.vector.tensor_copy(row_nof[:, :], row_no[:, :]).then_inc(row_no_ready, 1)

            def split_table(m):
                dve.wait_ge(hi_ready, m + 1)
                nc.vector.tensor_tensor(table_lo[:, m, :, :], table_raw[m % 2][:, :, :],
                                        table_hi[:, m, :, :].bitcast(fp32), ALU.subtract).then_inc(lo_ready, 1)

            def make_selection(turn, m, first):
                if m == 0:
                    dve.wait_ge(early_in, (turn + 1) * 16)
                if m == EARLY:
                    dve.wait_ge(late_in, (turn + 1) * 16)
                if not (first and m < 2):
                    back = 2 if m >= 2 else (1 + 2 * m if NMT % 2 else 2)
                    dve.wait_ge(looked_up, turn * NMT + (m - back + 1))
                ids = ids_early[:, m, :] if m < EARLY else ids_late[:, m - EARLY, :]
                for c in range(CV):
                    last = nc.vector.tensor_scalar(select[m % 2][:, c, :], ids, row_nof[:, c:c + 1], None, ALU.is_equal)
                last.then_inc(selected, 1)

            def keep_vectors(turn, u, first):
                for g in range(NG):
                    if by_act(u, g):
                        continue
                    dve.wait_ge(vec_made, turn * (U * NG) + (u * NG + g + 1))
                    nc.vector.tensor_copy(vecs[u][:, :, g * G4:(g + 1) * G4],
                                          vec_ps[fill_of(u, g) % 2][:, :].rearrange("p (v b) -> p b v", b=P)
                                          ).then_inc(kept_dve, 1)

            def turn_products(turn, u, first):
                dve.wait_ge(gram_made, turn * U + (u + 1))
                if not first:
                    dve.wait_ge(pairs_made, turn * U + (u - U + 1))
                src = gram_ps[:, :].rearrange("p (j m) -> p m j", m=PITCH)
                nc.vector.transpose(gram_b[u][:, 0:NV * PITCH], src[:, 0:NV, :])
                nc.vector.transpose(gram_b[u][:, NV * PITCH:], src[:, 0:KD, :]).then_inc(gram_kept, 1)
                dve.wait_ge(gram_kept, turn * U + (u + 1))
                picked = bass.AP(gram_b[u], PITCH, [[(NV + KD) * PITCH, P], [PITCH + 1, NV], [PITCH, KD]])
                nc.vector.tensor_copy(pairs_b[u][:, :].rearrange("p (n k) -> p n k", k=KD),
                                      picked).then_inc(pairs_picked, 1)

            def turn_all(turn, first, last):
                for m in range(EARLY, NMT):
                    if first:
                        split_table(m)
                    make_selection(turn, m, first)
                keep_vectors(turn, 0, first)
                turn_products(turn, 0, first)
                keep_vectors(turn, 1, first)
                if not last:
                    for m in range(EARLY):
                        make_selection(turn + 1, m, False)
                turn_products(turn, 1, first)

            dve.wait_ge(row_no_ready, 1)
            for m in range(EARLY):
                split_table(m)
                make_selection(0, m, True)
            turn_all(0, True, False)
            dve.wait_ge(weights_in, 7 * 16)
            nc.vector.tensor_tensor(w1s[:, :], w1d[:, :], w1e[:, :], ALU.add).then_inc(w1_summed, 1)
            with dve.Fori(1, TURNS - 1) as i:
                turn_all(i, False, False)
            turn_all(TURNS - 1, False, True)


def kernel(r_dense_proj, ids, W_top1, b_top1, W_top2, b_top2, W_top3, **tables):
    import concourse.bacc as bacc
    from concourse.bass_utils import run_bass_kernel_spmd

    nc = bacc.Bacc("TRN2", target_bir_lowering=False, num_devices=1)
    arrays = {}

    def given(name, a):
        a = np.ascontiguousarray(a)
        arrays[name] = a
        return nc.dram_tensor(name, a.shape, mybir.dt.from_np(a.dtype), kind="ExternalInput").ap()

    D = r_dense_proj.shape[1]
    W = np.asarray(W_top1)
    ids = np.asarray(ids)
    order = lookup_order([tables[f"tbl_{f}"].shape[0] for f in range(N_TABLES)])
    gather, matrix = order[:-N_MATRIX], order[-N_MATRIX:]
    args = [
        given("dense", r_dense_proj), given("ids_gather", ids[:, gather]), given("ids_matrix", ids[:, matrix].T),
        [given(f"tbl_{f}", tables[f"tbl_{f}"]) for f in gather],
        [given(f"tbl_{f}", tables[f"tbl_{f}"]) for f in matrix],
        given("w1_dense", W[0:D]), given("w1_pairs", W[pair_rows(D, order)]), given("w1_again", W[W.shape[0] - D:]),
        given("b1", b_top1), given("w2", W_top2), given("b2", b_top2), given("w3", W_top3),
    ]
    y = nc.dram_tensor("y", (r_dense_proj.shape[0], W_top3.shape[1]), mybir.dt.float32, kind="ExternalOutput").ap()
    dlrm_tower(nc, *args, y)
    r = run_bass_kernel_spmd(nc, [arrays], core_ids=[0])
    return r.results[0]["y"]
```

```python
import concourse.bass as bass
from concourse import mybir
from contextlib import ExitStack
import numpy as np

N_TABLES = 26
N_MATRIX = 8


def lookup_order(sizes):
    smallest = sorted(range(len(sizes)), key=lambda f: (sizes[f], f))[:N_MATRIX]
    return [f for f in range(len(sizes)) if f not in smallest] + smallest


def pair_rows(first_row, order):
    vector = [0] + [1 + f for f in order]
    n_vec = len(vector)
    rows, cols = np.triu_indices(n_vec, k=1)
    place = np.zeros((n_vec, n_vec), dtype=np.int64)
    place[rows, cols] = np.arange(len(rows))
    place[cols, rows] = np.arange(len(rows))
    return np.array([first_row + place[vector[n], vector[(n + k) % n_vec]]
                     for n in range(n_vec) for k in range(1, n_vec // 2 + 1)])


def dlrm_tower(nc, dense, ids_gather, ids_matrix, gather_tables, matrix_tables,
               w1_dense, w1_pairs, w1_again, b1, w2, b2, w3, y):
    fp32 = mybir.dt.float32
    fp32r = mybir.dt.float32r
    ALU = mybir.AluOpType
    ACT = mybir.ActivationFunctionType

    P = 128
    B, D = dense.shape
    NGT = len(gather_tables)
    NMT = len(matrix_tables)
    NT_ = 1 + NGT
    NV = NT_ + NMT
    PITCH = 32
    KD = NV // 2
    NC = 3
    KP = NV * KD // NC
    Q = 32
    NQ = P // Q
    U = 2
    UB = U * P
    TURNS = B // UB
    G4 = 4
    NG = -(-NT_ // G4)
    MG = -(-NMT // 2)
    KV = 125
    CV = [t.shape[0] // KV for t in matrix_tables]
    RING = 3
    EARLY = RING
    H1 = w1_dense.shape[1]
    H2 = w2.shape[1]
    C1, C2 = H1 // P, H2 // P
    assert all(t.shape[0] % KV == 0 for t in matrix_tables)
    groups = [list(range(g * G4, min(NT_, (g + 1) * G4))) for g in range(NG)]
    gathers = [len([v for v in g if v > 0]) for g in groups]

    ctx = ExitStack()
    with ctx:
        def sb(name, shape, dt=fp32):
            return ctx.enter_context(nc.sbuf_tensor(name, shape, dt))

        def pb(name, shape):
            return ctx.enter_context(nc.psum_tensor(name, shape, fp32))

        def sem(name):
            return ctx.enter_context(nc.semaphore(name))

        index = [sb(f"index{u}", [P, NGT], mybir.dt.int32) for u in range(U)]
        rows = [sb(f"rows{u}", [P, NT_ * D]) for u in range(U)]
        vecs = [sb(f"vecs{u}", [D, P, NV]) for u in range(U)]
        ids_early = sb("ids_early", [KV, EARLY, UB], mybir.dt.int32)
        ids_late = sb("ids_late", [KV, NMT - EARLY, UB], mybir.dt.int32)
        row_no = sb("row_no", [KV, 1], mybir.dt.int32)
        row_nof = sb("row_nof", [KV, 1])
        select = [sb(f"select{i}", [KV, max(CV[i::RING]), UB], fp32r) for i in range(RING)]
        staged = sb("staged", [P, 2 * max(CV) * D])
        RAW = max(CV) * D
        raw_at = [staged[0:KV, 0:RAW], staged[0:KV, RAW:2 * RAW],
                  rows[1][0:KV, D:D + CV[2] * D], rows[1][0:KV, D + CV[2] * D:D + (CV[2] + CV[3]) * D]]
        RAW_OF = [0, 1, 2, 3] + [m % 2 for m in range(4, NMT)]

        def table_raw(m):
            return raw_at[RAW_OF[m]][:, 0:CV[m] * D].rearrange("p (c d) -> p c d", d=D)

        table_hi = [sb(f"table_hi{m}", [KV, CV[m], D], fp32r) for m in range(NMT)]
        table_lo = [sb(f"table_lo{m}", [KV, CV[m], D], fp32r) for m in range(NMT)]
        GRAM = (NV + KD) * PITCH
        gram_b = sb("gram_b", [P, U * GRAM])
        assert C1 * UB + C2 * UB + U * NV * KD <= 2 * max(CV) * D
        h1_t = staged[:, 0:C1 * UB].rearrange("p (c b) -> p c b", b=UB)
        h2_t = staged[:, C1 * UB:(C1 + C2) * UB].rearrange("p (c b) -> p c b", b=UB)
        pairs_b = [staged[:, (C1 + C2) * UB + u * NV * KD:(C1 + C2) * UB + (u + 1) * NV * KD]
                   for u in range(U)]
        pairs_hi = sb("pairs_hi", [KP, NC, UB], fp32r)
        pairs_lo = sb("pairs_lo", [KP, NC, UB], fp32r)
        dense_hi = sb("dense_hi", [D, UB], fp32r)
        dense_lo = sb("dense_lo", [D, UB], fp32r)
        h1_hi = sb("h1_hi", [P, C1, UB], fp32r)
        h1_lo = sb("h1_lo", [P, C1, UB], fp32r)
        y_row = sb("y_row", [1, UB])
        ident = sb("ident", [P, P])
        w1d = sb("w1d", [D, H1])
        w1e = sb("w1e", [D, H1])
        assert NC * H1 + C1 * H2 <= U * GRAM
        w1p = gram_b[0:KP, 0:NC * H1].rearrange("p (c n) -> p c n", n=H1)
        w2s = gram_b[:, NC * H1:NC * H1 + C1 * H2].rearrange("p (c n) -> p c n", n=H2)
        w1s_hi = sb("w1s_hi", [D, H1], fp32r)
        w1s_lo = sb("w1s_lo", [D, H1], fp32r)
        w1p_hi = sb("w1p_hi", [KP, NC, H1], fp32r)
        w1p_lo = sb("w1p_lo", [KP, NC, H1], fp32r)
        w2_hi = sb("w2_hi", [P, C1, H2], fp32r)
        w2_lo = sb("w2_lo", [P, C1, H2], fp32r)
        w3s = sb("w3s", [P, C2])
        b1s = sb("b1s", [P, C1])
        b2s = sb("b2s", [P, C2])

        vec_ps = [pb(f"vec_ps{i}", [P, 512]) for i in range(3)]
        gram_ps = pb("gram_ps", [P, Q * PITCH])
        pair_ps = vec_ps[2]
        h1_ps = pb("h1_ps", [P, C1, UB])
        h2_ps = pb("h2_ps", [P, C2, UB])

        index_in = [sem(f"index_in{u}") for u in range(U)]
        dense_in = [sem(f"dense_in{u}") for u in range(U)]
        early_in = sem("early_in")
        late_in = sem("late_in")
        table_in = [sem(f"table_in{i}") for i in range(4)]
        gathered = [[sem(f"gathered{u}_{g}") for g in range(NG)] for u in range(U)]
        tiles_begun = sem("tiles_begun")
        weights_in = sem("weights_in")
        ident_zero = sem("ident_zero")
        ident_ready = sem("ident_ready")
        row_no_made = sem("row_no_made")
        row_no_ready = sem("row_no_ready")
        hi_ready = sem("hi_ready")
        lo_ready = sem("lo_ready")
        w1_summed = sem("w1_summed")
        weights_hi = sem("weights_hi")
        weights_lo = sem("weights_lo")
        ids_ahead = sem("ids_ahead")
        gram_cleared = sem("gram_cleared")
        selected = sem("selected")
        looked_up = sem("looked_up")
        looked_kept = sem("looked_kept")
        vec_made = sem("vec_made")
        kept_act = sem("kept_act")
        kept_dve = sem("kept_dve")
        gram_made = sem("gram_made")
        gram_kept = sem("gram_kept")
        pairs_picked = sem("pairs_picked")
        pairs_made = sem("pairs_made")
        pairs_high = sem("pairs_high")
        pairs_low = sem("pairs_low")
        dense_high = sem("dense_high")
        dense_low = sem("dense_low")
        h1_made = sem("h1_made")
        h1_kept = sem("h1_kept")
        h1_high = sem("h1_high")
        h1_low = sem("h1_low")
        h2_made = sem("h2_made")
        h2_kept = sem("h2_kept")
        y_made = sem("y_made")
        y_kept = sem("y_kept")
        y_out = sem("y_out")

        T_PER_TURN = U * NG
        LOOKED = [("M", g) for g in range(MG)]
        LOOKED_FIRST = LOOKED
        LOOKED_LATER = LOOKED[:2] + [("X", U - 1 - U)] + LOOKED[2:]
        T_FIRST = [("T", k) for k in range(NG)]
        T_SECOND = [("T", k) for k in range(NG, T_PER_TURN)]
        USUAL = LOOKED_LATER + T_FIRST + T_SECOND + [("X", 0)]
        IN_FIRST_TURN = LOOKED_FIRST + T_FIRST + T_SECOND + [("X", 0)]
        IN_LAST_TURN = USUAL + [("X", U - 1)]

        def bank_of(user):
            kind, n = user
            return {"M": n % 2, "T": n % 3, "X": 2}[kind]

        def by_act(k):
            return k % 2 == 0

        def groups_kept(engine_is_act, k):
            return len([i for i in range(k + 1) if by_act(i) == engine_is_act])

        PER_ACT = groups_kept(True, T_PER_TURN - 1)
        PER_DVE = groups_kept(False, T_PER_TURN - 1)

        def wait_emptied(pe, turn, user, turns_ago):
            kind, n = user
            if kind == "M":
                pe.wait_ge(looked_kept, turn * MG + (n + 1 - turns_ago * MG))
            elif kind == "X":
                pe.wait_ge(pairs_high, turn * U + (n + 1 - turns_ago * U))
                pe.wait_ge(pairs_low, turn * U + (n + 1 - turns_ago * U))
            elif by_act(n):
                pe.wait_ge(kept_act, turn * PER_ACT + (groups_kept(True, n) - turns_ago * PER_ACT))
            else:
                pe.wait_ge(kept_dve, turn * PER_DVE + (groups_kept(False, n) - turns_ago * PER_DVE))

        def wait_bank(pe, turn, user, first, last=False):
            users = IN_FIRST_TURN if first else IN_LAST_TURN if last else USUAL
            before = [x for x in users[:users.index(user)] if bank_of(x) == bank_of(user)]
            if before:
                wait_emptied(pe, turn, before[-1], 0)
            elif not first:
                wait_emptied(pe, turn, [x for x in USUAL if bank_of(x) == bank_of(user)][-1], 1)

        block = ctx.enter_context(nc.Block())

        ids_g = ids_gather.rearrange("(t p) f -> t p f", p=P)
        dense_rows = dense.rearrange("(t p) d -> t p d", p=P)
        y_rows = y.rearrange("(t b) o -> t o b", b=UB)
        TILE = [slice(u * P, (u + 1) * P) for u in range(U)]
        ids_m = ids_matrix.rearrange("f (t b) -> t f b", b=UB)

        def on_all(turn, lo, hi):
            return ids_m[turn, lo:hi, :].rearrange("f (o b) -> o f b", o=1).broadcast_to([KV, hi - lo, UB])

        @block.sync
        def _(sp):
            for u in range(U):
                sp.dma_start(index[u][:, :], ids_g[u, :, :]).then_inc(index_in[u], 16)
            sp.dma_start(ids_early[:, :, :], on_all(0, 0, EARLY)).then_inc(early_in, 16)
            for m in range(NMT):
                if m >= 4:
                    sp.wait_ge(lo_ready, max(n for n in range(m) if RAW_OF[n] == RAW_OF[m]) + 1)
                sp.dma_start(table_raw(m),
                             matrix_tables[m].rearrange("(c k) d -> k c d", k=KV)).then_inc(table_in[RAW_OF[m]], 16)
                if m == 3:
                    sp.dma_start(ids_late[:, :, :], on_all(0, EARLY, NMT)).then_inc(late_in, 16)
                    for u in range(U):
                        sp.dma_start(rows[u][:, 0:D], dense_rows[u, :, :]).then_inc(dense_in[u], 16)
            with sp.Fori(1, TURNS) as i:
                sp.wait_ge(selected, (i - 1) * NMT + EARLY)
                sp.dma_start(ids_early[:, :, :], on_all(i, 0, EARLY)).then_inc(early_in, 16)
                sp.wait_ge(selected, i * NMT)
                sp.dma_start(ids_late[:, :, :], on_all(i, EARLY, NMT)).then_inc(late_in, 16)
                for u in range(U):
                    sp.wait_ge(vec_made, (i * U + (u - U + 1)) * NG)
                    sp.dma_start(index[u][:, :], ids_g[i * U + u, :, :]).then_inc(index_in[u], 16)
                    sp.dma_start(rows[u][:, 0:D], dense_rows[i * U + u, :, :]).then_inc(dense_in[u], 16)

        @block.gpsimd
        def _(pool):
            nc.gpsimd.iota(row_no[:, :], pattern=[[0, 1]], base=0, channel_multiplier=1).then_inc(row_no_made, 1)
            nc.gpsimd.memset(ident[:, :], 0.0).then_inc(ident_zero, 1)
            pool.wait_ge(ident_zero, 1)
            nc.gpsimd.affine_select(out=ident[:, :], in_=ident[:, :], compare_op=ALU.not_equal, fill=1.0, base=0,
                                    pattern=[[-1, P]], channel_multiplier=1).then_inc(ident_ready, 1)

            def gather_tile(turn, u, first):
                if not first:
                    pool.wait_ge(vec_made, (turn * U + (u - U + 1)) * NG)
                pool.wait_ge(index_in[u], (turn + 1) * 16)
                pool.sem_inc(tiles_begun, 1)
                for g in range(NG):
                    for v in groups[g]:
                        if v > 0:
                            nc.gpsimd.indirect_dma_start(
                                out=rows[u][:, v * D:(v + 1) * D], out_offset=None, in_=gather_tables[v - 1][:, :],
                                in_offset=bass.IndirectOffsetOnAxis(ap=index[u][:, v - 1:v], axis=0),
                            ).then_inc(gathered[u][g], 16)

            gather_tile(0, 0, True)
            pool.wait_ge(lo_ready, 4)
            gather_tile(0, 1, True)
            with pool.Fori(1, TURNS) as i:
                for u in range(U):
                    gather_tile(i, u, False)

        @block.tensor
        def _(pe):
            def look_up(turn, group, first):
                wait_bank(pe, turn, ("M", group), first)
                for m in range(2 * group, min(2 * group + 2, NMT)):
                    if first:
                        pe.wait_ge(hi_ready, m + 1)
                        pe.wait_ge(lo_ready, m + 1)
                    pe.wait_ge(selected, turn * NMT + (m + 1))
                    out = vec_ps[bank_of(("M", group))][:, (m % 2) * UB:(m % 2 + 1) * UB]
                    for c in range(CV[m]):
                        nc.tensor.matmul(out, table_hi[m][:, c, :], select[m % RING][:, c, :], start=c == 0, stop=False)
                        last = nc.tensor.matmul(out, table_lo[m][:, c, :], select[m % RING][:, c, :], start=False,
                                                stop=c == CV[m] - 1)
                    last.then_inc(looked_up, 1)

            def tile_vectors(turn, u, first):
                for g in range(NG):
                    if g == 0:
                        pe.wait_ge(dense_in[u], (turn + 1) * 16)
                    pe.wait_ge(gathered[u][g], (turn + 1) * (16 * gathers[g]))
                    mine = ("T", u * NG + g)
                    wait_bank(pe, turn, mine, first)
                    for k, v in enumerate(groups[g]):
                        last = nc.tensor.transpose(vec_ps[bank_of(mine)][:, k * P:(k + 1) * P],
                                                   rows[u][:, v * D:(v + 1) * D], ident[:, :])
                    last.then_inc(vec_made, 1)

            def tile_gram(turn, u, first):
                pe.wait_ge(kept_act, turn * PER_ACT + groups_kept(True, u * NG + NG - 1))
                pe.wait_ge(kept_dve, turn * PER_DVE + groups_kept(False, u * NG + NG - 1))
                pe.wait_ge(looked_kept, (turn + 1) * MG)
                if not (first and u == 0):
                    pe.wait_ge(gram_kept, turn * U + u)
                for j in range(Q):
                    for q in range(NQ):
                        mine = vecs[u][:, q * Q + j, :]
                        last = nc.tensor.matmul(gram_ps[q * Q:q * Q + NV, j * PITCH:j * PITCH + NV], mine, mine,
                                                start=True, stop=True)
                last.then_inc(gram_made, 1)

            def tile_pairs(turn, tile, first, last_turn=False):
                u = tile % U
                pe.wait_ge(pairs_picked, turn * U + (tile + 1))
                wait_bank(pe, turn, ("X", tile), first, last_turn)
                for c in range(NC):
                    last = nc.tensor.transpose(pair_ps[0:KP, c * P:(c + 1) * P], pairs_b[u][:, c * KP:(c + 1) * KP],
                                               ident[:, :])
                last.then_inc(pairs_made, 1)

            def products(out, w_hi, w_lo, x_hi, x_lo, start, stop):
                nc.tensor.matmul(out, w_hi, x_lo, start=start, stop=False)
                nc.tensor.matmul(out, w_lo, x_hi, start=False, stop=False)
                return nc.tensor.matmul(out, w_hi, x_hi, start=False, stop=stop)

            def layer1(turn, first):
                for part in (pairs_high, pairs_low, dense_high, dense_low):
                    pe.wait_ge(part, (turn + 1) * U)
                if not first:
                    pe.wait_ge(h1_kept, turn * C1)
                for o in range(C1):
                    out, rows_o = h1_ps[:, o, :], slice(o * P, (o + 1) * P)
                    products(out, w1s_hi[:, rows_o], w1s_lo[:, rows_o], dense_hi[:, :], dense_lo[:, :], True, False)
                    for c in range(NC):
                        last = products(out, w1p_hi[:, c, rows_o], w1p_lo[:, c, rows_o], pairs_hi[:, c, :],
                                        pairs_lo[:, c, :], False, c == NC - 1)
                    last.then_inc(h1_made, 1)

            def layer2(turn, first):
                if not first:
                    pe.wait_ge(y_kept, turn)
                pe.wait_ge(h1_high, (turn + 1) * (C1 // 2))
                pe.wait_ge(h1_low, (turn + 1) * (C1 // 2))
                for o in range(C2):
                    rows_o = slice(o * P, (o + 1) * P)
                    for c in range(C1):
                        last = products(h2_ps[:, o, :], w2_hi[:, c, rows_o], w2_lo[:, c, rows_o], h1_hi[:, c, :],
                                        h1_lo[:, c, :], c == 0, c == C1 - 1)
                    last.then_inc(h2_made, 1)

            def layer3(turn):
                pe.wait_ge(h2_kept, (turn + 1) * C2)
                for c in range(C2):
                    last = nc.tensor.matmul(h2_ps[0:1, 0, :], w3s[:, c:c + 1], h2_t[:, c, :], start=c == 0,
                                            stop=c == C2 - 1)
                last.then_inc(y_made, 1)

            def turn_all(turn, before, first, second):
                for group in range(MG):
                    look_up(turn, group, first)
                    if group == 1 and not first:
                        tile_pairs(turn, -1, False)
                tile_vectors(turn, 0, first)
                if not first:
                    layer1(before, second)
                tile_gram(turn, 0, first)
                if not first:
                    layer2(before, second)
                tile_vectors(turn, 1, first)
                tile_pairs(turn, 0, first)
                if not first:
                    layer3(before)
                tile_gram(turn, 1, first)

            pe.wait_ge(ident_ready, 1)
            pe.wait_ge(gram_cleared, 1)
            turn_all(0, None, True, False)
            pe.wait_ge(weights_hi, 3)
            pe.wait_ge(weights_lo, 3)
            turn_all(1, 0, False, True)
            with pe.Fori(2, TURNS) as i:
                turn_all(i, i - 1, False, False)
            tile_pairs(TURNS - 1, U - 1, False, True)
            layer1(TURNS - 1, False)
            layer2(TURNS - 1, False)
            layer3(TURNS - 1)

        @block.scalar
        def _(act):
            def load_weights():
                act.dma_start(w1d[:, :], w1_dense[:, :]).then_inc(weights_in, 16)
                act.dma_start(w1e[:, :], w1_again[:, :]).then_inc(weights_in, 16)
                act.dma_start(w1p, w1_pairs.rearrange("(c k) n -> k c n", k=KP)).then_inc(weights_in, 16)
                act.dma_start(w2s, w2.rearrange("(c k) n -> k c n", k=P)).then_inc(weights_in, 16)
                with nc.allow_non_contiguous_dma(reason="small columns, once"):
                    act.dma_start(w3s[:, :], w3.rearrange("(c k) o -> k (c o)", k=P)).then_inc(weights_in, 16)
                    act.dma_start(b1s[:, :], b1.rearrange("(c k) -> k c", k=P)).then_inc(weights_in, 16)
                    act.dma_start(b2s[:, :], b2.rearrange("(c k) -> k c", k=P)).then_inc(weights_in, 16)

            def raise_table(m):
                act.wait_ge(table_in[RAW_OF[m]], RAW_OF[:m + 1].count(RAW_OF[m]) * 16)
                nc.scalar.copy(table_hi[m][:, :, :], table_raw(m)).then_inc(hi_ready, 1)

            def keep_looked_up(turn, group, first):
                n = min(2, NMT - 2 * group)
                act.wait_ge(looked_up, turn * NMT + (2 * group + n))
                if group == 0 and not first:
                    act.wait_ge(gram_made, turn * U)
                at = NT_ + 2 * group
                for u in range(U):
                    src = vec_ps[bank_of(("M", group))][:, 0:n * UB].rearrange("p (m u b) -> p u b m", u=U, b=P)
                    last = nc.scalar.copy(vecs[u][:, :, at:at + n], src[:, u])
                last.then_inc(looked_kept, 1)

            def keep_pairs(turn, u):
                act.wait_ge(pairs_made, turn * U + (u + 1))
                nc.scalar.copy(pairs_hi[:, :, TILE[u]],
                               pair_ps[0:KP, 0:NC * P].rearrange("p (c b) -> p c b", b=P)).then_inc(pairs_high, 1)

            def keep_vectors(turn, u):
                for g in range(NG):
                    k = u * NG + g
                    bank = vec_ps[bank_of(("T", k))]
                    if not by_act(k):
                        continue
                    act.wait_ge(vec_made, turn * (U * NG) + (u * NG + g + 1))
                    n = len(groups[g])
                    nc.scalar.copy(vecs[u][:, :, g * G4:g * G4 + n],
                                   bank[:, 0:n * P].rearrange("p (v b) -> p b v", b=P)).then_inc(kept_act, 1)

            def keep_dense(turn, u):
                act.wait_ge(kept_act, turn * PER_ACT + groups_kept(True, u * NG + NG - 1))
                act.wait_ge(kept_dve, turn * PER_DVE + groups_kept(False, u * NG + NG - 1))
                nc.scalar.copy(dense_hi[:, TILE[u]], vecs[u][:, :, 0]).then_inc(dense_high, 1)

            def relu1(turn, first):
                if not first:
                    act.wait_ge(h2_made, turn * C2)
                for o in range(C1):
                    act.wait_ge(h1_made, turn * C1 + (o // 2 * 2 + 2))
                    nc.scalar.activation(h1_t[:, o, :], h1_ps[:, o, :], ACT.Relu,
                                         bias=b1s[:, o:o + 1]).then_inc(h1_kept, 1)
                    if o % 2:
                        act.wait_ge(h1_kept, turn * C1 + (o + 1))
                        nc.scalar.copy(h1_hi[:, o - 1:o + 1, :], h1_t[:, o - 1:o + 1, :]).then_inc(h1_high, 1)

            def relu2(turn, first):
                if not first:
                    act.wait_ge(y_made, turn)
                act.wait_ge(h2_made, (turn + 1) * C2)
                for o in range(C2):
                    nc.scalar.activation(h2_t[:, o, :], h2_ps[:, o, :], ACT.Relu,
                                         bias=b2s[:, o:o + 1]).then_inc(h2_kept, 1)

            def give_y(turn, first):
                act.wait_ge(y_made, turn + 1)
                if not first:
                    act.wait_ge(y_out, turn * 16)
                nc.scalar.copy(y_row[:, :], h2_ps[0:1, 0, :]).then_inc(y_kept, 1)
                act.wait_ge(y_kept, turn + 1)
                act.dma_start(y_rows[turn, :, :], y_row[:, :]).then_inc(y_out, 16)

            def turn_all(turn, before, first, second):
                for group in range(MG):
                    keep_looked_up(turn, group, first)
                    if first and group == 0:
                        for m in range(6, NMT):
                            raise_table(m)
                    if first and group == 1:
                        act.wait_ge(weights_in, 7 * 16)
                        nc.scalar.copy(w1p_hi[:, :, :], w1p).then_inc(weights_hi, 1)
                        nc.scalar.copy(w2_hi[:, :, :], w2s).then_inc(weights_hi, 1)
                    if group == 1 and not first:
                        keep_pairs(before, U - 1)
                if first:
                    act.wait_ge(w1_summed, 1)
                    nc.scalar.copy(w1s_hi[:, :], w1d[:, :]).then_inc(weights_hi, 1)
                keep_vectors(turn, 0)
                if not first:
                    relu1(before, second)
                keep_dense(turn, 0)
                if not first:
                    relu2(before, second)
                keep_vectors(turn, 1)
                keep_dense(turn, 1)
                keep_pairs(turn, 0)
                if not first:
                    give_y(before, second)

            for m in range(6):
                raise_table(m)
                if m == 3:
                    load_weights()
            turn_all(0, None, True, False)
            turn_all(1, 0, False, True)
            with act.Fori(2, TURNS) as i:
                turn_all(i, i - 1, False, False)
            keep_pairs(TURNS - 1, U - 1)
            relu1(TURNS - 1, False)
            relu2(TURNS - 1, False)
            give_y(TURNS - 1, False)
            act.wait_ge(y_out, TURNS * 16)

        @block.vector
        def _(dve):
            nc.vector.memset(gram_ps[:, :], 0.0).then_inc(gram_cleared, 1)
            dve.wait_ge(row_no_made, 1)
            nc.vector.tensor_copy(row_nof[:, :], row_no[:, :]).then_inc(row_no_ready, 1)

            def split_table(m):
                dve.wait_ge(hi_ready, m + 1)
                nc.vector.tensor_tensor(table_lo[m][:, :, :], table_raw(m),
                                        table_hi[m][:, :, :].bitcast(fp32), ALU.subtract).then_inc(lo_ready, 1)

            def make_ahead(turn, late):
                half = ids_late if late else ids_early
                dve.wait_ge(late_in if late else early_in, (turn + 1) * 16)
                nc.vector.tensor_scalar(half[:, :, :], half[:, :, :], row_nof[:, 0:1],
                                        None, ALU.subtract).then_inc(ids_ahead, 1)

            def make_selection(turn, m, first):
                if m in (0, EARLY):
                    late = int(m == EARLY)
                    make_ahead(turn, late)
                    dve.wait_ge(ids_ahead, turn * 2 + (late + 1))
                if m >= RING:
                    dve.wait_ge(looked_up, turn * NMT + (m - RING + 1))
                elif not first:
                    last_user = max(n for n in range(NMT) if n % RING == m % RING)
                    dve.wait_ge(looked_up, turn * NMT + (last_user + 1 - NMT))
                ids = ids_early[:, m, :] if m < EARLY else ids_late[:, m - EARLY, :]
                for c in range(CV[m]):
                    last = nc.vector.tensor_scalar(select[m % RING][:, c, :], ids, float(c * KV), None, ALU.is_equal)
                last.then_inc(selected, 1)

            def lower_pairs(turn, u):
                dve.wait_ge(pairs_high, turn * U + (u + 1))
                nc.vector.tensor_tensor(pairs_lo[:, :, TILE[u]], pair_ps[0:KP, 0:NC * P].rearrange("p (c b) -> p c b", b=P),
                                        pairs_hi[:, :, TILE[u]].bitcast(fp32), ALU.subtract).then_inc(pairs_low, 1)

            def lower_dense(turn, u):
                dve.wait_ge(dense_high, turn * U + (u + 1))
                nc.vector.tensor_tensor(dense_lo[:, TILE[u]], vecs[u][:, :, 0], dense_hi[:, TILE[u]].bitcast(fp32),
                                        ALU.subtract).then_inc(dense_low, 1)

            def lower_h1(turn):
                for bank in range(C1 // 2):
                    two = slice(2 * bank, 2 * bank + 2)
                    dve.wait_ge(h1_high, turn * (C1 // 2) + (bank + 1))
                    nc.vector.tensor_tensor(h1_lo[:, two, :], h1_t[:, two, :], h1_hi[:, two, :].bitcast(fp32),
                                            ALU.subtract).then_inc(h1_low, 1)

            def sum_weights():
                dve.wait_ge(weights_in, 7 * 16)
                nc.vector.tensor_tensor(w1d[:, :], w1d[:, :], w1e[:, :], ALU.add).then_inc(w1_summed, 1)

            def split_weights():
                for n, (lo, hi, w) in enumerate(((w1p_lo[:, :, :], w1p_hi[:, :, :], w1p), (w2_lo[:, :, :], w2_hi[:, :, :], w2s),
                                                 (w1s_lo[:, :], w1s_hi[:, :], w1d[:, :]))):
                    dve.wait_ge(weights_hi, n + 1)
                    nc.vector.tensor_tensor(lo, w, hi.bitcast(fp32), ALU.subtract).then_inc(weights_lo, 1)

            def keep_vectors(turn, u, first):
                for g in range(NG):
                    if by_act(u * NG + g):
                        continue
                    dve.wait_ge(vec_made, turn * (U * NG) + (u * NG + g + 1))
                    n = len(groups[g])
                    nc.vector.tensor_copy(vecs[u][:, :, g * G4:g * G4 + n],
                                          vec_ps[bank_of(("T", u * NG + g))][:, 0:n * P].rearrange("p (v b) -> p b v", b=P)
                                          ).then_inc(kept_dve, 1)

            def turn_products(turn, u, first):
                dve.wait_ge(gram_made, turn * U + (u + 1))
                if not first:
                    dve.wait_ge(pairs_made, turn * U + (u - U + 1))
                src = gram_ps[:, :].rearrange("p (j m) -> p m j", m=PITCH)
                nc.vector.transpose(gram_b[:, u * GRAM:u * GRAM + NV * PITCH], src[:, 0:NV, :])
                nc.vector.transpose(gram_b[:, u * GRAM + NV * PITCH:(u + 1) * GRAM], src[:, 0:KD, :]).then_inc(gram_kept, 1)
                dve.wait_ge(gram_kept, turn * U + (u + 1))
                picked = bass.AP(gram_b, u * GRAM + PITCH, [[U * GRAM, P], [PITCH + 1, NV], [PITCH, KD]])
                nc.vector.tensor_copy(pairs_b[u].rearrange("p (n k) -> p n k", k=KD),
                                      picked).then_inc(pairs_picked, 1)

            def turn_all(turn, before, first, last):
                for m in range(EARLY, NMT):
                    if first and m >= 4:
                        split_table(m)
                    if first and m == NMT - 1:
                        sum_weights()
                    make_selection(turn, m, first)
                if not first:
                    lower_pairs(before, U - 1)
                keep_vectors(turn, 0, first)
                if first:
                    split_weights()
                    dve.wait_ge(weights_lo, 3)
                    turn_products(turn, 0, first)
                    lower_dense(turn, 0)
                    keep_vectors(turn, 1, first)
                    for m in range(EARLY):
                        make_selection(turn + 1, m, False)
                    lower_dense(turn, 1)
                    lower_pairs(turn, 0)
                else:
                    if not last:
                        for m in range(2):
                            make_selection(turn + 1, m, False)
                    lower_h1(before)
                    lower_dense(turn, 0)
                    if not last:
                        make_selection(turn + 1, EARLY - 1, False)
                    turn_products(turn, 0, first)
                    keep_vectors(turn, 1, first)
                    lower_dense(turn, 1)
                    lower_pairs(turn, 0)
                turn_products(turn, 1, first)

            dve.wait_ge(row_no_ready, 1)
            make_selection(0, 0, True)
            split_table(0)
            split_table(1)
            make_selection(0, 1, True)
            split_table(2)
            make_selection(0, 2, True)
            split_table(3)
            turn_all(0, None, True, False)
            with dve.Fori(1, TURNS - 1) as i:
                turn_all(i, i - 1, False, False)
            turn_all(TURNS - 1, TURNS - 2, False, True)
            lower_pairs(TURNS - 1, U - 1)
            lower_h1(TURNS - 1)


def kernel(r_dense_proj, ids, W_top1, b_top1, W_top2, b_top2, W_top3, **tables):
    import concourse.bacc as bacc
    from concourse.bass_utils import run_bass_kernel_spmd

    nc = bacc.Bacc("TRN2", target_bir_lowering=False, num_devices=1, dynamic_dma_scratch_size=8192)
    arrays = {}

    def given(name, a):
        a = np.ascontiguousarray(a)
        arrays[name] = a
        return nc.dram_tensor(name, a.shape, mybir.dt.from_np(a.dtype), kind="ExternalInput").ap()

    D = r_dense_proj.shape[1]
    W = np.asarray(W_top1)
    ids = np.asarray(ids)
    order = lookup_order([tables[f"tbl_{f}"].shape[0] for f in range(N_TABLES)])
    gather, matrix = order[:-N_MATRIX], order[-N_MATRIX:]
    args = [
        given("dense", r_dense_proj), given("ids_gather", ids[:, gather]), given("ids_matrix", ids[:, matrix].T),
        [given(f"tbl_{f}", tables[f"tbl_{f}"]) for f in gather],
        [given(f"tbl_{f}", tables[f"tbl_{f}"]) for f in matrix],
        given("w1_dense", W[0:D]), given("w1_pairs", W[pair_rows(D, order)]), given("w1_again", W[W.shape[0] - D:]),
        given("b1", b_top1), given("w2", W_top2), given("b2", b_top2), given("w3", W_top3),
    ]
    y = nc.dram_tensor("y", (r_dense_proj.shape[0], W_top3.shape[1]), mybir.dt.float32, kind="ExternalOutput").ap()
    dlrm_tower(nc, *args, y)
    r = run_bass_kernel_spmd(nc, [arrays], core_ids=[0])
    return r.results[0]["y"]
```
